# Optimizing a Trainium2 kernel written in Bass

```python
import numpy as np
import jax
import jax.numpy as jnp

def _softmax(x, axis=-1):
    return jax.nn.softmax(x, axis=axis)

def _gelu(x):
    return jax.nn.gelu(x, approximate=True)

def _silu(x):
    return jax.nn.silu(x)

def _sigmoid(x):
    return jax.nn.sigmoid(x)

def _layernorm(x, axis=-1, eps=1e-05):
    m = jnp.mean(x, axis=axis, keepdims=True)
    v = jnp.var(x, axis=axis, keepdims=True)
    return (x - m) / jnp.sqrt(v + eps)

def _scatter_add(tgt, idx, src, axis=0):
    return tgt.at[idx].add(src)

def _segment_sum(src, seg, n):
    return jax.ops.segment_sum(src, seg, n)
kernel_name = 'mk_adj_resnorm_d1_adj_r2_9a4d7a'

def setup_inputs(seed: int=0):
    np.random.seed(seed)
    _w = jnp.asarray

    def _rec_inputs():
        import jax
        import jax.numpy as jnp
        _gk = jax.random.key(seed)
        x = -0.0005207 + 1.001 * jax.random.normal(jax.random.fold_in(_gk, 1), (8, 1024, 64), jnp.float32)
        _a = jax.random.bernoulli(jax.random.fold_in(_gk, 2), 0.0078125, (1024, 1024))
        _a = jnp.logical_or(_a, jnp.swapaxes(_a, -1, -2))
        _a = jnp.logical_or(_a, jnp.eye(1024, dtype=bool))
        _af = _a.astype(jnp.float32)
        _af = _af * jax.random.uniform(jax.random.fold_in(_gk, 3), (1024, 1024), jnp.float32, 0.05, 1)
        adj = _af
        return (x, adj)
    x, adj = _rec_inputs()

    def _L0_gnn_setup():
        import jax, jax.numpy as jnp
        import numpy as np
        B, N, C_IN, C_OUT = (16, 1024, 64, 64)
        key = jax.random.key(seed)
        ks = jax.random.split(key, 7)
        scale = 1.0 / np.sqrt(C_IN)
        return {'x': jax.random.normal(ks[0], (B, N, C_IN), dtype=jnp.float32), 'adj': jax.random.uniform(ks[1], (N, N), dtype=jnp.float32), 'Wq': jax.random.normal(ks[2], (C_OUT, C_IN), dtype=jnp.float32) * scale, 'bq': jax.random.normal(ks[3], (C_OUT,), dtype=jnp.float32) * scale, 'Wk': jax.random.normal(ks[4], (C_OUT, C_IN), dtype=jnp.float32) * scale, 'bk': jax.random.normal(ks[5], (C_OUT,), dtype=jnp.float32) * scale, 'Wv': jax.random.normal(ks[6], (C_OUT, C_IN), dtype=jnp.float32) * scale}
    _L0_gnn_all = _L0_gnn_setup()
    _L0_gnn_in = {k: v for k, v in _L0_gnn_all.items() if k in ('Wq', 'bq', 'Wk', 'bk', 'Wv')}
    del _L0_gnn_all
    return {'x': x, 'adj': adj, 'L0_gnn_Wq': _L0_gnn_in['Wq'], 'L0_gnn_bq': _L0_gnn_in['bq'], 'L0_gnn_Wk': _L0_gnn_in['Wk'], 'L0_gnn_bk': _L0_gnn_in['bk'], 'L0_gnn_Wv': _L0_gnn_in['Wv']}

def reference(x, adj, L0_gnn_Wq, L0_gnn_bq, L0_gnn_Wk, L0_gnn_bk, L0_gnn_Wv):
    import jax
    import jax.numpy as jnp

    def _L0_gnn_ref(x, adj, Wq, bq, Wk, bk, Wv):
        import jax, jax.numpy as jnp
        import numpy as np
        B, N, C_IN, C_OUT = (16, 1024, 64, 64)
        Q = jnp.einsum('bnc,oc->bno', x, Wq) + bq
        K = jnp.einsum('bnc,oc->bno', x, Wk) + bk
        V = jnp.einsum('bnc,oc->bno', x, Wv)
        score = jnp.einsum('bnc,bmc->bnm', Q, K)
        score = jax.nn.softmax(score, axis=1)
        score = jnp.einsum('bnm,mc->bnc', score, adj)
        out = jnp.einsum('bnm,bmc->bnc', score, V)
        return out
    x = _layernorm(x + _L0_gnn_ref(x, adj, L0_gnn_Wq, L0_gnn_bq, L0_gnn_Wk, L0_gnn_bk, L0_gnn_Wv), axis=-1)
    return x

_drawn_inputs = setup_inputs


def setup_inputs(seed=0):
    import zlib

    import numpy as np

    out = dict(_drawn_inputs(seed))
    spreads = {}
    factors = {}
    for name, (base, spread) in spreads.items():
        noise = np.random.default_rng([zlib.crc32(name.encode()), seed]).standard_normal(out[name].shape)
        drawn = base * np.exp(spread * noise) if base else spread * noise
        out[name] = jnp.asarray(drawn.astype(out[name].dtype))
    for name, factor in factors.items():
        out[name] = (out[name] * factor).astype(out[name].dtype)
    return out
```

```python
from contextlib import ExitStack

import concourse.bass as bass
from concourse import mybir

F32 = mybir.dt.float32
F32R = mybir.dt.float32r
ALU = mybir.AluOpType
ACT = mybir.ActivationFunctionType
AX_X = mybir.AxisListType.X

B, N, C = 8, 1024, 64
P = 128
NCH = N // P
BANK = 512
HALVES = N // BANK
STEPS = NCH // 2
EPS = 1e-5

SCORE_BUFS = 2
Y_BANKS = 2
RAW_ADJ = 4
ADJ_BUFS = 2

HEAD = 2


def bits(ap):
    return ap.bitcast(F32)


def gnn_resnorm_kernel(nc: bass.Bass, xT, xn, adjT, wqT, bq, wkT, bk, wvT, out):
    ctx = ExitStack()
    with ctx:
        def sb(name, shape, dt=F32):
            return ctx.enter_context(nc.sbuf_tensor(name, shape, dt))

        def pb(name, shape):
            return ctx.enter_context(nc.psum_tensor(name, shape, F32))

        def sem(name):
            return ctx.enter_context(nc.semaphore(name))

        w_raw = sb("w_raw", [P, 2, P])
        w_high = sb("w_high", [P, 2, P], F32R)
        w_low = sb("w_low", [P, 2, P], F32R)
        wv = sb("wv", [P, P])
        bias = sb("bias", [P, 2])
        x_raw = sb("x_raw", [P, N])
        x_split = sb("x_split", [P, N], F32R)
        q_high = sb("q_high", [P, N], F32R)
        q_low = sb("q_low", [P, N], F32R)
        k_split = sb("k_split", [P, N], F32R)
        x_nodes = sb("x_nodes", [P, NCH, B * C])
        xn_high = sb("xn_high", [P, NCH, B * C], F32R)
        xn_low = sb("xn_low", [P, NCH, B * C], F32R)
        adj_raw = sb("adj_raw", [P, RAW_ADJ, NCH * P])
        adj_high = sb("adj_high", [P, ADJ_BUFS, NCH * P], F32R)
        adj_low = sb("adj_low", [P, ADJ_BUFS, NCH * P], F32R)
        ax = sb("ax", [P, NCH, B * C])
        ax_scaled = sb("ax_scaled", [P, 2, NCH, C])
        probs = sb("probs", [P, 2, NCH, N])
        neg_max = sb("neg_max", [P, 2, NCH])
        sums = sb("sums", [P, 2, NCH])
        recip = sb("recip", [P, 2, NCH])
        agg = sb("agg", [P, N])
        y = sb("y", [P, NCH, C])
        cent = sb("cent", [P, NCH, C])
        square = sb("square", [P, NCH, C])
        normed = sb("normed", [P, NCH, C])
        y_sum = sb("y_sum", [P, NCH])
        neg_mean = sb("neg_mean", [P, NCH])
        sq_sum = sb("sq_sum", [P, NCH])
        var_eps = sb("var_eps", [P, NCH])
        rstd = sb("rstd", [P, NCH])
        neg_half = sb("neg_half", [P, NCH])
        start_mark = sb("start_mark", [P, 16])

        scores = [pb(f"scores{i}", [P, N]) for i in range(SCORE_BUFS)]
        acc = pb("acc", [P, N])
        misc = pb("misc", [P, N])

        w_landed = sem("w_landed")
        x_landed = sem("x_landed")
        xn_landed = [sem(f"xn_landed{i}") for i in range(4)]
        adj_landed = [sem(f"adj_landed{i}") for i in range(RAW_ADJ)]
        out_stored = sem("out_stored")
        q_projected = sem("q_projected")
        k_projected = sem("k_projected")
        scores_ready = sem("scores_ready")
        ax_ready = sem("ax_ready")
        aggregated = sem("aggregated")
        mixed = sem("mixed")
        w_rounded = sem("w_rounded")
        x_rounded = sem("x_rounded")
        xn_rounded = sem("xn_rounded")
        adj_rounded = sem("adj_rounded")
        q_rounded = sem("q_rounded")
        k_rounded = sem("k_rounded")
        exp_done = sem("exp_done")
        agg_copied = sem("agg_copied")
        w_split = sem("w_split")
        q_split = sem("q_split")
        k_split_done = sem("k_split_done")
        max_done = sem("max_done")
        ax_copied = sem("ax_copied")
        recip_done = sem("recip_done")
        residual_added = sem("residual_added")
        summed = sem("summed")
        mean_done = sem("mean_done")
        var_summed = sem("var_summed")
        var_done = sem("var_done")
        rstd_done = sem("rstd_done")
        xn_split_v = sem("xn_split_v")
        constant_set = sem("constant_set")
        x_split_done = sem("x_split_done")
        xn_split_g = sem("xn_split_g")
        adj_split = sem("adj_split")
        ax_divided = sem("ax_divided")
        centered = sem("centered")
        squared = sem("squared")
        normalized = sem("normalized")

        XN_PARTS = len(xn_landed)
        XN_K = NCH // XN_PARTS

        FROM_ONE = (k_split_done, residual_added, agg_copied, scores_ready, mixed, centered,
                    aggregated, normalized, out_stored)

        def after(count):
            return count + 1

        def exp_count(batch, chunks):
            return batch * NCH + (chunks + SCORE_BUFS)

        def ax_count(group):
            return group + (1 + Y_BANKS)

        block = ctx.enter_context(nc.Block())

        @block.sync
        def _(sp):
            def load_x(batch):
                for half in range(2):
                    sp.dma_start(x_raw[half * C:(half + 1) * C, :], xT[batch]).then_inc(x_landed, 16)

            def load_adj(j):
                if j >= RAW_ADJ:
                    sp.wait_ge(adj_split, j - RAW_ADJ + 1)
                sp.dma_start(adj_raw[:, j % RAW_ADJ, :], adjT[j]).then_inc(adj_landed[j % RAW_ADJ], 16)

            load_x(0)
            for part in range(XN_PARTS):
                ks = slice(part * XN_K, (part + 1) * XN_K)
                sp.dma_start(x_nodes[:, ks, :], xn[:, ks, :]).then_inc(xn_landed[part], 16)
            for j in range(RAW_ADJ):
                load_adj(j)
            for b in range(1, HEAD + 1):
                sp.wait_ge(x_split_done, b)
                load_x(b)
            for j in range(RAW_ADJ, NCH):
                load_adj(j)

            def store(b):
                sp.wait_ge(normalized, after(b + 1))
                sp.dma_start(out[b], normed[:, :, :]).then_inc(out_stored, 16)

            with sp.Fori(0, (B - HEAD) // 2) as i:
                for par in range(2):
                    b = i * 2 + par
                    sp.wait_ge(x_split_done, b + HEAD + 1)
                    load_x((b + HEAD + 1) % B)
                    store(b)
            for b in range(B - HEAD, B):
                store(b)
            sp.wait_ge(out_stored, after(16 * B))
            sp.wait_ge(x_landed, 32 * (B + 1))

        @block.tensor
        def _(pe):
            def project(batch):
                pe.wait_ge(x_split_done, batch + 1)
                for w, done in ((0, q_projected), (1, k_projected)):
                    for h in range(HALVES):
                        if w == 0:
                            pe.wait_ge(k_split_done, after(batch * HALVES))
                        else:
                            pe.wait_ge(q_split, batch * HALVES + (h + 1))
                        cols = slice(h * BANK, (h + 1) * BANK)
                        nc.tensor.matmul(misc[:, cols], w_high[:, w, :], x_split[:, cols],
                                         start=True, stop=False)
                        nc.tensor.matmul(misc[:, cols], w_low[:, w, :], x_split[:, cols],
                                         start=False, stop=True).then_inc(done, 1)
                    if w == 0:
                        yield

            def score(batch, u):
                if u == 0:
                    pe.wait_ge(q_split, batch * HALVES + HALVES)
                    pe.wait_ge(k_split_done, after(batch * HALVES + HALVES))
                for s in range(2):
                    j = 2 * u + s
                    pe.wait_ge(exp_done, exp_count(batch, j + 1 - SCORE_BUFS))
                    for h in range(HALVES):
                        cols = slice(h * BANK, (h + 1) * BANK)
                        keys = k_split[:, j * P:(j + 1) * P]
                        nc.tensor.matmul(scores[s][:, cols], keys, q_high[:, cols],
                                         start=True, stop=False)
                        last = nc.tensor.matmul(scores[s][:, cols], keys, q_low[:, cols],
                                                start=False, stop=True)
                    last.then_inc(scores_ready, 1)

            def adj_times_x(group, u):
                pe.wait_ge(adj_split, group + 1)
                pe.wait_ge(ax_copied, group + 1)
                rows = acc[:, (u % Y_BANKS) * BANK:(u % Y_BANKS + 1) * BANK]
                a, b = adj_high[:, u % ADJ_BUFS, :], adj_low[:, u % ADJ_BUFS, :]
                for k in range(NCH):
                    ms = slice(k * P, (k + 1) * P)
                    nc.tensor.matmul(rows, a[:, ms], xn_high[:, k, :], start=(k == 0), stop=False)
                    nc.tensor.matmul(rows, a[:, ms], xn_low[:, k, :], start=False, stop=False)
                    last = nc.tensor.matmul(rows, b[:, ms], xn_high[:, k, :], start=False,
                                            stop=(k == NCH - 1))
                last.then_inc(ax_ready, 1)

            def aggregate(b, par, u):
                if u == 0:
                    pe.wait_ge(ax_divided, b + 1)
                    pe.wait_ge(exp_done, exp_count(b, NCH))
                    pe.wait_ge(agg_copied, after(b))
                for h in range(HALVES):
                    for s in range(2):
                        last = nc.tensor.matmul(
                            acc[s * C:(s + 1) * C, h * BANK:(h + 1) * BANK],
                            ax_scaled[:, par, 2 * u + s, :],
                            probs[:, par, 2 * u + s, h * BANK:(h + 1) * BANK],
                            start=(u == 0), stop=(u == STEPS - 1))
                last.then_inc(aggregated, 1)

            def mix(b):
                pe.wait_ge(agg_copied, after(b + 1))
                for k in range(NCH):
                    last = nc.tensor.matmul(misc[:, k * P:(k + 1) * P], agg[:, k * P:(k + 1) * P],
                                            wv[:, :], start=True, stop=True)
                last.then_inc(mixed, 1)

            pe.wait_ge(w_split, 1)
            with pe.Fori(0, HEAD) as b:
                for _ in project(b):
                    pass
                score(b, 0)
                pe.wait_ge(xn_split_v, 2)
                pe.wait_ge(xn_split_g, 2)
                for u in range(STEPS):
                    adj_times_x(b * STEPS + u, u)
                    if u + 1 < STEPS:
                        score(b, u + 1)

            pe.wait_ge(ax_copied, ax_count(NCH - 1))
            with pe.Fori(0, (B - HEAD) // 2) as i:
                for par in range(2):
                    b = i * 2 + par
                    pe.wait_ge(residual_added, after(b))
                    projection = project(b + HEAD)
                    next(projection)
                    aggregate(b, par, 0)
                    for _ in projection:
                        pass
                    aggregate(b, par, 1)
                    score(b + HEAD, 0)
                    aggregate(b, par, 2)
                    score(b + HEAD, 1)
                    aggregate(b, par, 3)
                    score(b + HEAD, 2)
                    pe.wait_ge(k_split_done, after((b + HEAD + 1) * HALVES))
                    mix(b)
                    score(b + HEAD, 3)
            for b in range(B - HEAD, B):
                for u in range(STEPS):
                    aggregate(b, b % 2, u)
                pe.wait_ge(residual_added, after(b))
                mix(b)

        @block.scalar
        def _(act):
            for w, (mat, vec) in enumerate(((wqT, bq), (wkT, bk))):
                for r in range(2):
                    for c in range(2):
                        act.dma_start(w_raw[r * C:(r + 1) * C, w, c * C:(c + 1) * C], mat).then_inc(w_landed, 16)
                    act.dma_start(bias[r * C:(r + 1) * C, w:w + 1], vec).then_inc(w_landed, 16)
            for r in range(2):
                for c in range(2):
                    act.dma_start(wv[r * C:(r + 1) * C, c * C:(c + 1) * C], wvT).then_inc(w_landed, 16)

            def round_x(batch, first=False):
                act.wait_ge(x_landed, batch * 32 + 32)
                if not first:
                    act.wait_ge(k_projected, batch * HALVES)
                nc.scalar.activation(x_split[:, :], x_raw[:, :], ACT.Copy).then_inc(x_rounded, 1)

            def round_q(batch):
                for h in range(HALVES):
                    cols = slice(h * BANK, (h + 1) * BANK)
                    act.wait_ge(q_projected, batch * HALVES + (h + 1))
                    act.wait_ge(scores_ready, after(batch * NCH))
                    nc.scalar.activation(q_high[:, cols], misc[:, cols], ACT.Identity,
                                         bias=bias[:, 0:1]).then_inc(q_rounded, 1)

            def round_k(batch):
                for h in range(HALVES):
                    cols = slice(h * BANK, (h + 1) * BANK)
                    act.wait_ge(k_projected, batch * HALVES + (h + 1))
                    nc.scalar.activation(k_split[:, cols], misc[:, cols], ACT.Identity,
                                         bias=bias[:, 1:2]).then_inc(k_rounded, 1)

            def exps(batch, par, u, aggregating=None):
                if aggregating is not None:
                    act.wait_ge(aggregated, after(aggregating * STEPS + (u + 1)))
                for s in range(2):
                    j = 2 * u + s
                    act.wait_ge(max_done, batch * NCH + (j + 1))
                    nc.scalar.activation(probs[:, par, j, :], scores[s][:, :], ACT.Exp,
                                         bias=neg_max[:, par, j:j + 1],
                                         accum_out=sums[:, par, j:j + 1]).then_inc(exp_done, 1)

            act.wait_ge(w_landed, 16 * 16)
            nc.scalar.activation(w_high[:, :, :], w_raw[:, :, :], ACT.Copy).then_inc(w_rounded, 1)
            round_x(0, first=True)
            for part in range(XN_PARTS):
                act.wait_ge(xn_landed[part], 16)
                ks = slice(part * XN_K, (part + 1) * XN_K)
                nc.scalar.activation(xn_high[:, ks, :], x_nodes[:, ks, :], ACT.Copy).then_inc(xn_rounded, 1)

            with act.Fori(0, HEAD) as b:
                round_q(b)
                round_k(b)
                for u in range(STEPS):
                    act.wait_ge(adj_landed[u], b * 16 + 16)
                    act.wait_ge(ax_copied, b * STEPS + (u + 1))
                    nc.scalar.activation(adj_high[:, u % ADJ_BUFS, :], adj_raw[:, u, :],
                                         ACT.Copy).then_inc(adj_rounded, 1)
                    exps(b, b, u)
                    if u == 1:
                        round_x(b + 1)

            with act.Fori(0, (B - HEAD) // 2) as i:
                for par in range(2):
                    b = i * 2 + par
                    round_q(b + HEAD)
                    round_k(b + HEAD)
                    exps(b + HEAD, par, 0, b)
                    round_x(b + HEAD + 1)
                    exps(b + HEAD, par, 1, b)
                    act.wait_ge(aggregated, after(b * STEPS + STEPS))
                    act.wait_ge(mixed, after(b))
                    nc.scalar.activation(agg[:, :], acc[:, :], ACT.Copy).then_inc(agg_copied, 1)
                    exps(b + HEAD, par, 2, b)
                    exps(b + HEAD, par, 3, b)
            for b in range(B - HEAD, B):
                act.wait_ge(aggregated, after(b * STEPS + STEPS))
                act.wait_ge(mixed, after(b))
                nc.scalar.activation(agg[:, :], acc[:, :], ACT.Copy).then_inc(agg_copied, 1)

        @block.vector
        def _(dve):
            starts = [exp_done] * SCORE_BUFS + [ax_copied] * Y_BANKS + list(FROM_ONE)
            for n, semaphore in enumerate(starts):
                nc.vector.memset(start_mark[:, n:n + 1], 0.0).then_inc(semaphore, 1)

            def split_q(batch):
                for h in range(HALVES):
                    cols = slice(h * BANK, (h + 1) * BANK)
                    dve.wait_ge(q_rounded, batch * HALVES + (h + 1))
                    nc.vector.scalar_tensor_tensor(
                        out=q_low[:, cols], in0=misc[:, cols], scalar=bias[:, 0:1],
                        in1=bits(q_high[:, cols]), op0=ALU.add, op1=ALU.subtract).then_inc(q_split, 1)

            def split_k(batch):
                for h in range(HALVES):
                    cols = slice(h * BANK, (h + 1) * BANK)
                    dve.wait_ge(k_rounded, batch * HALVES + (h + 1))
                    nc.vector.scalar_tensor_tensor(
                        out=k_split[C:P, cols], in0=misc[C:P, cols], scalar=bias[C:P, 1:2],
                        in1=bits(k_split[C:P, cols]), op0=ALU.add, op1=ALU.subtract).then_inc(k_split_done, 1)

            def maxima(batch, par, u):
                for s in range(2):
                    j = 2 * u + s
                    dve.wait_ge(scores_ready, after(batch * NCH + (j + 1)))
                    nc.vector.tensor_reduce(neg_max[:, par, j:j + 1], scores[s][:, :], AX_X, ALU.max,
                                            negate=True).then_inc(max_done, 1)

            def reciprocals(batch, par):
                dve.wait_ge(exp_done, exp_count(batch, NCH))
                nc.vector.reciprocal(recip[:, par, :], sums[:, par, :]).then_inc(recip_done, 1)

            def residual_and_mean(b):
                dve.wait_ge(mixed, after(b + 1))
                dve.wait_ge(centered, after(b))
                nc.vector.tensor_tensor(y[:, :, :], misc[:, :].rearrange("p (k c) -> p k c", k=NCH)[:, :, 0:C],
                                        x_nodes[:, :, bass.ds(b * C, C)], ALU.add).then_inc(residual_added, 1)
                dve.wait_ge(residual_added, after(b + 1))
                nc.vector.tensor_reduce(y_sum[:, :], y[:, :, :], AX_X, ALU.add).then_inc(summed, 1)
                dve.wait_ge(summed, b + 1)
                nc.vector.tensor_scalar(neg_mean[:, :], y_sum[:, :], -1.0 / C, None, ALU.mult).then_inc(mean_done, 1)

            def inverse_deviation(b):
                dve.wait_ge(squared, b + 1)
                nc.vector.tensor_reduce(sq_sum[:, :], square[:, :, :], AX_X, ALU.add).then_inc(var_summed, 1)
                dve.wait_ge(var_summed, b + 1)
                nc.vector.tensor_scalar(var_eps[:, :], sq_sum[:, :], 1.0 / C, EPS, ALU.mult, ALU.add).then_inc(var_done, 1)

            dve.wait_ge(w_rounded, 1)
            nc.vector.tensor_tensor(w_low[:, :, :], w_raw[:, :, :], bits(w_high[:, :, :]), ALU.subtract).then_inc(w_split, 1)
            for part in range(XN_PARTS // 2):
                dve.wait_ge(xn_rounded, part + 1)
                ks = slice(part * XN_K, (part + 1) * XN_K)
                nc.vector.tensor_tensor(xn_low[:, ks, :], x_nodes[:, ks, :], bits(xn_high[:, ks, :]),
                                        ALU.subtract).then_inc(xn_split_v, 1)

            with dve.Fori(0, HEAD) as b:
                split_q(b)
                split_k(b)
                for u in range(STEPS):
                    maxima(b, b, u)
                    dve.wait_ge(ax_ready, b * STEPS + (u + 1))
                    nc.vector.tensor_copy(ax[:, b * STEPS + u, :],
                                          acc[:, (u % Y_BANKS) * BANK:(u % Y_BANKS + 1) * BANK]).then_inc(ax_copied, 1)

            reciprocals(0, 0)
            with dve.Fori(0, (B - HEAD) // 2) as i:
                for par in range(2):
                    b = i * 2 + par
                    split_q(b + HEAD)
                    split_k(b + HEAD)
                    reciprocals(b + 1, 1 - par)
                    maxima(b + HEAD, par, 0)
                    maxima(b + HEAD, par, 1)
                    maxima(b + HEAD, par, 2)
                    residual_and_mean(b)
                    maxima(b + HEAD, par, 3)
                    inverse_deviation(b)
            for b in range(B - HEAD, B):
                if b + 1 < B:
                    reciprocals(b + 1, (b + 1) % 2)
                residual_and_mean(b)
                inverse_deviation(b)

        @block.gpsimd
        def _(pool):
            def split_x(batch):
                pool.wait_ge(x_rounded, batch + 1)
                nc.gpsimd.tensor_tensor(x_split[C:P, :], x_raw[C:P, :], bits(x_split[C:P, :]),
                                        ALU.subtract).then_inc(x_split_done, 1)
                pool.wait_ge(x_split_done, batch + 1)

            def divide_ax(b, par):
                pool.wait_ge(recip_done, b + 1)
                nc.gpsimd.tensor_tensor(ax_scaled[:, par, :, :], ax[:, :, bass.ds(b * C, C)],
                                        recip[:, par, :].unsqueeze(2).broadcast_to([P, NCH, C]),
                                        ALU.mult).then_inc(ax_divided, 1)

            def center_and_square(b):
                pool.wait_ge(mean_done, b + 1)
                pool.wait_ge(normalized, after(b))
                nc.gpsimd.tensor_tensor(cent[:, :, :], y[:, :, :],
                                        neg_mean[:, :].unsqueeze(2).broadcast_to([P, NCH, C]),
                                        ALU.add).then_inc(centered, 1)
                pool.wait_ge(centered, after(b + 1))
                nc.gpsimd.tensor_tensor(square[:, :, :], cent[:, :, :], cent[:, :, :], ALU.mult).then_inc(squared, 1)

            def normalize(b):
                pool.wait_ge(var_done, b + 1)
                nc.gpsimd.tensor_tensor(rstd[:, :], var_eps[:, :], neg_half[:, :], ALU.pow).then_inc(rstd_done, 1)
                pool.wait_ge(rstd_done, b + 1)
                pool.wait_ge(out_stored, after(b * 16))
                nc.gpsimd.tensor_tensor(normed[:, :, :], cent[:, :, :],
                                        rstd[:, :].unsqueeze(2).broadcast_to([P, NCH, C]),
                                        ALU.mult).then_inc(normalized, 1)

            nc.gpsimd.memset(neg_half[:, :], -0.5).then_inc(constant_set, 1)
            pool.wait_ge(constant_set, 1)
            split_x(0)
            for part in range(XN_PARTS // 2, XN_PARTS):
                pool.wait_ge(xn_rounded, part + 1)
                ks = slice(part * XN_K, (part + 1) * XN_K)
                nc.gpsimd.tensor_tensor(xn_low[:, ks, :], x_nodes[:, ks, :], bits(xn_high[:, ks, :]),
                                        ALU.subtract).then_inc(xn_split_g, 1)
            with pool.Fori(0, HEAD) as b:
                for u in range(STEPS):
                    pool.wait_ge(adj_rounded, b * STEPS + (u + 1))
                    nc.gpsimd.tensor_tensor(adj_low[:, u % ADJ_BUFS, :], adj_raw[:, u, :],
                                            bits(adj_high[:, u % ADJ_BUFS, :]), ALU.subtract).then_inc(adj_split, 1)
                    if u == 1:
                        pool.wait_ge(adj_split, b * STEPS + (u + 1))
                        split_x(b + 1)
            pool.wait_ge(ax_copied, ax_count(NCH - 1))
            divide_ax(0, 0)
            with pool.Fori(0, (B - HEAD) // 2) as i:
                for par in range(2):
                    b = i * 2 + par
                    pool.wait_ge(aggregated, after(b * STEPS))
                    divide_ax(b + 1, 1 - par)
                    pool.wait_ge(ax_divided, b + 2)
                    split_x(b + HEAD + 1)
                    center_and_square(b)
                    normalize(b)
            for b in range(B - HEAD, B):
                if b + 1 < B:
                    pool.wait_ge(aggregated, after(b * STEPS))
                    divide_ax(b + 1, (b + 1) % 2)
                center_and_square(b)
                normalize(b)


def kernel(x, adj, L0_gnn_Wq, L0_gnn_bq, L0_gnn_Wk, L0_gnn_bk, L0_gnn_Wv):
    import numpy as np
    import concourse.bacc as bacc
    from concourse.bass_utils import run_bass_kernel_spmd

    def laid(a):
        return np.ascontiguousarray(a)

    x, adj = np.asarray(x), np.asarray(adj)
    arrays = {
        "xT": laid(x.transpose(0, 2, 1)),
        "xn": laid(x.reshape(B, NCH, P, C).transpose(2, 1, 0, 3).reshape(P, NCH, B * C)),
        "adjT": laid(adj.reshape(NCH, P, NCH, P).transpose(0, 3, 2, 1).reshape(NCH, P, NCH * P)),
        "wqT": laid(np.asarray(L0_gnn_Wq).T),
        "bq": laid(np.asarray(L0_gnn_bq).reshape(C, 1)),
        "wkT": laid(np.asarray(L0_gnn_Wk).T),
        "bk": laid(np.asarray(L0_gnn_bk).reshape(C, 1)),
        "wvT": laid(np.asarray(L0_gnn_Wv).T),
    }
    nc = bacc.Bacc("TRN2", target_bir_lowering=False, num_devices=1)
    args = [nc.dram_tensor(name, a.shape, mybir.dt.from_np(a.dtype), kind="ExternalInput").ap()
            for name, a in arrays.items()]
    out = nc.dram_tensor("out", (B, P, NCH * C), F32, kind="ExternalOutput").ap()
    gnn_resnorm_kernel(nc, *args, out)
    r = run_bass_kernel_spmd(nc, [arrays], core_ids=[0])
    got = r.results[0]["out"]
    return laid(got.reshape(B, P, NCH, C).transpose(0, 2, 1, 3).reshape(B, N, C))
```

```python
from contextlib import ExitStack

import concourse.bass as bass
from concourse import mybir

F32 = mybir.dt.float32
F32R = mybir.dt.float32r
ALU = mybir.AluOpType
ACT = mybir.ActivationFunctionType
AX_X = mybir.AxisListType.X

B, N, C = 8, 1024, 64
P = 128
NCH = N // P
BANK = 512
HALVES = N // BANK
STEPS = NCH // 2
EPS = 1e-5

SCORE_BUFS = 2
Y_BANKS = 2
RAW_ADJ = 2
ADJ_BUFS = 2

HEAD = 2
LOOPED = B - HEAD - 2


def bits(ap):
    return ap.bitcast(F32)


def gnn_resnorm_kernel(nc: bass.Bass, xT, xn, adjT, w_all, out):
    ctx = ExitStack()
    with ctx:
        def sb(name, shape, dt=F32):
            return ctx.enter_context(nc.sbuf_tensor(name, shape, dt))

        def pb(name, shape):
            return ctx.enter_context(nc.psum_tensor(name, shape, F32))

        def sem(name):
            return ctx.enter_context(nc.semaphore(name))

        weights = sb("weights", [P, 3 * P + 2])
        w_raw = weights[:, 0:2 * P].rearrange("p (w c) -> p w c", w=2)
        wv = weights[:, 2 * P:3 * P]
        bias = weights[:, 3 * P:3 * P + 2]
        w_high = sb("w_high", [P, 2, P], F32R)
        w_low = sb("w_low", [P, 2, P], F32R)
        x_raw = sb("x_raw", [P, N])
        x_split = sb("x_split", [P, N], F32R)
        q_high = sb("q_high", [P, 2, N], F32R)
        q_low = sb("q_low", [P, 2, N], F32R)
        k_split = sb("k_split", [P, 2, N], F32R)
        x_nodes = sb("x_nodes", [P, NCH, B * C])
        xn_high = sb("xn_high", [P, NCH, B * C], F32R)
        xn_low = sb("xn_low", [P, NCH, B * C], F32R)
        adj_raw = sb("adj_raw", [P, RAW_ADJ, NCH * P])
        adj_high = sb("adj_high", [P, ADJ_BUFS, NCH * P], F32R)
        adj_low = sb("adj_low", [P, ADJ_BUFS, NCH * P], F32R)
        ax = sb("ax", [P, NCH, B * C])
        ax_scaled = sb("ax_scaled", [P, 2, NCH, C])
        probs = sb("probs", [P, 2, NCH, N])
        neg_max = sb("neg_max", [P, 2, NCH])
        sums = sb("sums", [P, 2, NCH])
        recip = sb("recip", [P, 2, NCH])
        agg = sb("agg", [P, N])
        y = sb("y", [P, NCH, C])
        cent = sb("cent", [P, NCH, C])
        normed = sb("normed", [P, NCH, C])
        stats = sb("stats", [P, NCH, 6])
        moments = sb("moments", [P, NCH, 2])
        var_eps = sb("var_eps", [P, NCH])
        rstd = sb("rstd", [P, NCH])
        neg_half = sb("neg_half", [P, NCH])
        start_mark = sb("start_mark", [P, 16])

        scores = [pb(f"scores{i}", [P, N]) for i in range(SCORE_BUFS)]
        acc = pb("acc", [P, N])
        misc = pb("misc", [P, N])

        xn_split = [sem(f"xn_split{i}") for i in range(4)]
        w_landed = sem("w_landed")
        x_landed = sem("x_landed")
        xn_landed = [sem(f"xn_landed{i}") for i in range(4)]
        adj_landed = [sem(f"adj_landed{i}") for i in range(RAW_ADJ)]
        out_stored = sem("out_stored")
        q_projected = sem("q_projected")
        k_projected = sem("k_projected")
        scores_ready = sem("scores_ready")
        ax_ready = sem("ax_ready")
        aggregated = sem("aggregated")
        mixed = sem("mixed")
        w_rounded = sem("w_rounded")
        x_rounded = sem("x_rounded")
        xn_rounded = [sem(f"xn_rounded{i}") for i in range(4)]
        adj_rounded = sem("adj_rounded")
        q_rounded = sem("q_rounded")
        k_rounded = sem("k_rounded")
        exp_done = sem("exp_done")
        agg_copied = sem("agg_copied")
        w_split = sem("w_split")
        q_split = sem("q_split")
        k_split_done = sem("k_split_done")
        max_done = sem("max_done")
        ax_copied = sem("ax_copied")
        recip_done = sem("recip_done")
        residual_added = sem("residual_added")
        stats_done = sem("stats_done")
        moments_done = sem("moments_done")
        var_done = sem("var_done")
        rstd_done = sem("rstd_done")
        constant_set = sem("constant_set")
        x_split_done = sem("x_split_done")
        adj_split = sem("adj_split")
        ax_divided = sem("ax_divided")
        centered = sem("centered")
        normalized = sem("normalized")

        XN_PARTS = len(xn_landed)
        XN_K = NCH // XN_PARTS

        FROM_ONE = (k_split_done, residual_added, agg_copied, scores_ready, mixed, centered,
                    aggregated, normalized, out_stored)

        def after(count):
            return count + 1

        def exp_count(batch, chunks):
            return batch * NCH + (chunks + SCORE_BUFS)

        def ax_count(group):
            return group + (1 + Y_BANKS)

        block = ctx.enter_context(nc.Block())

        @block.sync
        def _(sp):
            def load_x(batch):
                for half in range(2):
                    sp.dma_start(x_raw[half * C:(half + 1) * C, :], xT[batch]).then_inc(x_landed, 16)

            def load_adj(j):
                if j >= RAW_ADJ:
                    sp.wait_ge(adj_split, j - RAW_ADJ + 1)
                sp.dma_start(adj_raw[:, j % RAW_ADJ, :], adjT[j]).then_inc(adj_landed[j % RAW_ADJ], 16)

            load_x(0)
            for part in range(XN_PARTS):
                ks = slice(part * XN_K, (part + 1) * XN_K)
                sp.dma_start(x_nodes[:, ks, :], xn[:, ks, :]).then_inc(xn_landed[part], 16)
            for j in range(NCH):
                load_adj(j)
                x_ahead = {1: 1, 3: 2, 5: 3}.get(j)
                if x_ahead:
                    sp.wait_ge(x_split_done, x_ahead)
                    load_x(x_ahead)

            def store(b):
                sp.wait_ge(normalized, after(b + 1))
                sp.dma_start(out[b], normed[:, :, :]).then_inc(out_stored, 16)

            with sp.Fori(0, LOOPED // 2) as i:
                for par in range(2):
                    b = i * 2 + par
                    sp.wait_ge(x_split_done, b + HEAD + 2)
                    load_x(b + HEAD + 2)
                    store(b)
            for b in range(LOOPED, B):
                store(b)
            sp.wait_ge(out_stored, after(16 * B))

        @block.tensor
        def _(pe):
            def project(batch, w, into):
                pe.wait_ge(x_split_done, batch + 1)
                for h in range(HALVES):
                    if w == 0:
                        pe.wait_ge(k_split_done, after(batch * HALVES))
                        done = q_projected
                    else:
                        if into is misc:
                            pe.wait_ge(q_split, batch * HALVES + (h + 1))
                        done = k_projected
                    cols = slice(h * BANK, (h + 1) * BANK)
                    nc.tensor.matmul(into[:, cols], w_high[:, w, :], x_split[:, cols],
                                     start=True, stop=False)
                    nc.tensor.matmul(into[:, cols], w_low[:, w, :], x_split[:, cols],
                                     start=False, stop=True).then_inc(done, 1)

            def score(batch, par, u):
                if u == 0:
                    pe.wait_ge(q_split, batch * HALVES + HALVES)
                    pe.wait_ge(k_split_done, after(batch * HALVES + HALVES))
                for s in range(2):
                    j = 2 * u + s
                    pe.wait_ge(exp_done, exp_count(batch, j + 1 - SCORE_BUFS))
                    for h in range(HALVES):
                        cols = slice(h * BANK, (h + 1) * BANK)
                        keys = k_split[:, par, j * P:(j + 1) * P]
                        nc.tensor.matmul(scores[s][:, cols], keys, q_high[:, par, cols],
                                         start=True, stop=False)
                        last = nc.tensor.matmul(scores[s][:, cols], keys, q_low[:, par, cols],
                                                start=False, stop=True)
                    last.then_inc(scores_ready, 1)

            def adj_times_x(group, u):
                pe.wait_ge(adj_split, group + 1)
                if group < Y_BANKS:
                    pe.wait_ge(k_split_done, after(group + 1))
                pe.wait_ge(ax_copied, group + 1)
                rows = acc[:, (u % Y_BANKS) * BANK:(u % Y_BANKS + 1) * BANK]
                a, b = adj_high[:, u % ADJ_BUFS, :], adj_low[:, u % ADJ_BUFS, :]
                for k in range(NCH):
                    if group == 0 and k % XN_K == 0:
                        pe.wait_ge(xn_split[k // XN_K], 1)
                    ms = slice(k * P, (k + 1) * P)
                    nc.tensor.matmul(rows, a[:, ms], xn_high[:, k, :], start=(k == 0), stop=False)
                    nc.tensor.matmul(rows, a[:, ms], xn_low[:, k, :], start=False, stop=False)
                    last = nc.tensor.matmul(rows, b[:, ms], xn_high[:, k, :], start=False,
                                            stop=(k == NCH - 1))
                last.then_inc(ax_ready, 1)

            def aggregate(b, par, u):
                if u == 0:
                    pe.wait_ge(ax_divided, b + 1)
                    pe.wait_ge(exp_done, exp_count(b, NCH))
                    pe.wait_ge(agg_copied, after(b))
                for h in range(HALVES):
                    for s in range(2):
                        last = nc.tensor.matmul(
                            acc[s * C:(s + 1) * C, h * BANK:(h + 1) * BANK],
                            ax_scaled[:, par, 2 * u + s, :],
                            probs[:, par, 2 * u + s, h * BANK:(h + 1) * BANK],
                            start=(u == 0), stop=(u == STEPS - 1))
                last.then_inc(aggregated, 1)

            def mix(b):
                pe.wait_ge(agg_copied, after(b + 1))
                for k in range(NCH):
                    last = nc.tensor.matmul(misc[:, k * P:(k + 1) * P], agg[:, k * P:(k + 1) * P],
                                            wv, start=True, stop=True)
                last.then_inc(mixed, 1)

            pe.wait_ge(w_split, 1)
            project(0, 0, misc)
            project(0, 1, acc)
            score(0, 0, 0)
            score(0, 0, 1)
            for b in range(HEAD):
                for u in range(STEPS):
                    adj_times_x(b * STEPS + u, u)
                    if u == 0:
                        project(b + 1, 0, misc)
                    if u == 1:
                        project(b + 1, 1, misc)
                    ahead = b * STEPS + u + 2
                    if ahead < HEAD * STEPS - 1:
                        score(ahead // STEPS, ahead // STEPS, ahead % STEPS)
            score(HEAD - 1, HEAD - 1, STEPS - 1)

            pe.wait_ge(ax_copied, ax_count(NCH - 1))

            def batch(b, par, scoring, projecting):
                for u in range(STEPS):
                    aggregate(b, par, u)
                    if projecting and u == 0:
                        pe.wait_ge(residual_added, after(b))
                        project(b + HEAD + 1, 0, misc)
                    if projecting and u == 1:
                        project(b + HEAD + 1, 1, misc)
                    if scoring:
                        score(b + HEAD, par, u)
                if projecting:
                    pe.wait_ge(k_split_done, after((b + HEAD + 2) * HALVES))
                else:
                    pe.wait_ge(residual_added, after(b))
                mix(b)

            with pe.Fori(0, LOOPED // 2) as i:
                for par in range(2):
                    batch(i * 2 + par, par, True, True)
            for b in range(LOOPED, B):
                batch(b, b % 2, b + HEAD < B, b + HEAD + 1 < B)

        @block.scalar
        def _(act):
            act.dma_start(weights[:, :], w_all).then_inc(w_landed, 16)

            def round_x(batch):
                act.wait_ge(x_landed, batch * 32 + 32)
                if not isinstance(batch, int) or batch > 0:
                    act.wait_ge(k_projected, batch * HALVES)
                nc.scalar.activation(x_split[:, :], x_raw[:, :], ACT.Copy).then_inc(x_rounded, 1)

            def round_q(batch, par):
                for h in range(HALVES):
                    cols = slice(h * BANK, (h + 1) * BANK)
                    act.wait_ge(q_projected, batch * HALVES + (h + 1))
                    if not isinstance(batch, int) or batch > 1:
                        act.wait_ge(scores_ready, after((batch - 1) * NCH))
                    nc.scalar.activation(q_high[:, par, cols], misc[:, cols], ACT.Identity,
                                         bias=bias[:, 0:1]).then_inc(q_rounded, 1)

            def round_k(batch, par, source):
                for h in range(HALVES):
                    cols = slice(h * BANK, (h + 1) * BANK)
                    act.wait_ge(k_projected, batch * HALVES + (h + 1))
                    nc.scalar.activation(k_split[:, par, cols], source[:, cols], ACT.Identity,
                                         bias=bias[:, 1:2]).then_inc(k_rounded, 1)

            def round_xn(part):
                act.wait_ge(xn_landed[part], 16)
                ks = slice(part * XN_K, (part + 1) * XN_K)
                nc.scalar.activation(xn_high[:, ks, :], x_nodes[:, ks, :], ACT.Copy).then_inc(xn_rounded[part], 1)

            def round_adj(group):
                act.wait_ge(adj_landed[group % RAW_ADJ], 16 * (group // RAW_ADJ + 1))
                act.wait_ge(ax_copied, group + 1)
                nc.scalar.activation(adj_high[:, group % ADJ_BUFS, :], adj_raw[:, group % RAW_ADJ, :],
                                     ACT.Copy).then_inc(adj_rounded, 1)

            def exps(batch, par, u, aggregating=None):
                if aggregating is not None:
                    act.wait_ge(aggregated, after(aggregating * STEPS + (u + 1)))
                for s in range(2):
                    j = 2 * u + s
                    act.wait_ge(max_done, batch * NCH + (j + 1))
                    nc.scalar.activation(probs[:, par, j, :], scores[s][:, :], ACT.Exp,
                                         bias=neg_max[:, par, j:j + 1],
                                         accum_out=sums[:, par, j:j + 1]).then_inc(exp_done, 1)

            act.wait_ge(w_landed, 16)
            nc.scalar.activation(w_high[:, :, :], w_raw, ACT.Copy).then_inc(w_rounded, 1)
            round_x(0)
            round_xn(0)
            round_q(0, 0)
            round_xn(2)
            round_k(0, 0, acc)
            round_xn(3)
            round_adj(0)
            exps(0, 0, 0)
            round_x(1)
            round_adj(1)
            exps(0, 0, 1)
            for b in range(HEAD):
                for u in range(STEPS):
                    if b * STEPS + u + 2 < NCH:
                        round_adj(b * STEPS + u + 2)
                    if u == 0:
                        round_q(b + 1, (b + 1) % 2)
                    if u == 1:
                        round_k(b + 1, (b + 1) % 2, misc)
                    if u == 2:
                        round_x(b + 2)
                    ahead = b * STEPS + u + 2
                    if ahead < HEAD * STEPS - 1:
                        exps(ahead // STEPS, ahead // STEPS, ahead % STEPS)
            exps(HEAD - 1, HEAD - 1, STEPS - 1)

            def batch(b, par, scoring, projecting, splitting):
                for u in range(STEPS):
                    if u == STEPS - 1:
                        act.wait_ge(aggregated, after(b * STEPS + STEPS))
                        act.wait_ge(mixed, after(b))
                        nc.scalar.activation(agg[:, :], acc[:, :], ACT.Copy).then_inc(agg_copied, 1)
                    if projecting and u == 0:
                        round_q(b + HEAD + 1, 1 - par)
                    if projecting and u == 1:
                        round_k(b + HEAD + 1, 1 - par, misc)
                    if splitting and u == 2:
                        round_x(b + HEAD + 2)
                    if scoring:
                        exps(b + HEAD, par, u, b)

            with act.Fori(0, LOOPED // 2) as i:
                for par in range(2):
                    batch(i * 2 + par, par, True, True, True)
            for b in range(LOOPED, B):
                batch(b, b % 2, b + HEAD < B, b + HEAD + 1 < B, b + HEAD + 2 < B)

        @block.vector
        def _(dve):
            starts = [exp_done] * SCORE_BUFS + [ax_copied] * Y_BANKS + list(FROM_ONE)
            for n, semaphore in enumerate(starts):
                nc.vector.memset(start_mark[:, n:n + 1], 0.0).then_inc(semaphore, 1)

            def split_q(batch, par):
                for h in range(HALVES):
                    cols = slice(h * BANK, (h + 1) * BANK)
                    dve.wait_ge(q_rounded, batch * HALVES + (h + 1))
                    nc.vector.scalar_tensor_tensor(
                        out=q_low[:, par, cols], in0=misc[:, cols], scalar=bias[:, 0:1],
                        in1=bits(q_high[:, par, cols]), op0=ALU.add, op1=ALU.subtract).then_inc(q_split, 1)

            def split_k(batch, par, source):
                for h in range(HALVES):
                    cols = slice(h * BANK, (h + 1) * BANK)
                    dve.wait_ge(k_rounded, batch * HALVES + (h + 1))
                    nc.vector.scalar_tensor_tensor(
                        out=k_split[C:P, par, cols], in0=source[C:P, cols], scalar=bias[C:P, 1:2],
                        in1=bits(k_split[C:P, par, cols]), op0=ALU.add, op1=ALU.subtract).then_inc(k_split_done, 1)

            def maxima(batch, par, u):
                for s in range(2):
                    j = 2 * u + s
                    dve.wait_ge(scores_ready, after(batch * NCH + (j + 1)))
                    nc.vector.tensor_reduce(neg_max[:, par, j:j + 1], scores[s][:, :], AX_X, ALU.max,
                                            negate=True).then_inc(max_done, 1)

            def reciprocals(batch, par):
                dve.wait_ge(exp_done, exp_count(batch, NCH))
                nc.vector.reciprocal(recip[:, par, :], sums[:, par, :]).then_inc(recip_done, 1)

            def residual_and_moments(b):
                dve.wait_ge(mixed, after(b + 1))
                dve.wait_ge(centered, after(b))
                nc.vector.tensor_tensor(y[:, :, :], misc[:, :].rearrange("p (k c) -> p k c", k=NCH)[:, :, 0:C],
                                        x_nodes[:, :, bass.ds(b * C, C)], ALU.add).then_inc(residual_added, 1)
                dve.wait_ge(residual_added, after(b + 1))
                for k in range(NCH):
                    last = nc.vector.bn_stats(stats[:, k, :], y[:, k, :])
                last.then_inc(stats_done, 1)
                dve.wait_ge(stats_done, b + 1)
                nc.vector.memset(start_mark[:, 0:1], 0.0)
                for k in range(NCH):
                    last = nc.vector.bn_aggr(moments[:, k, :], stats[:, k, :])
                last.then_inc(moments_done, 1)
                dve.wait_ge(moments_done, b + 1)
                dve.wait_ge(normalized, after(b))
                nc.vector.tensor_scalar(var_eps[:, :], moments[:, :, 1], EPS, None, ALU.add).then_inc(var_done, 1)

            def split_x(batch):
                dve.wait_ge(x_rounded, batch + 1)
                nc.vector.tensor_tensor(x_split[C:P, :], x_raw[C:P, :], bits(x_split[C:P, :]),
                                        ALU.subtract).then_inc(x_split_done, 1)

            def split_xn(part):
                ks = slice(part * XN_K, (part + 1) * XN_K)
                dve.wait_ge(xn_rounded[part], 1)
                nc.vector.tensor_tensor(xn_low[:, ks, :], x_nodes[:, ks, :], bits(xn_high[:, ks, :]),
                                        ALU.subtract).then_inc(xn_split[part], 1)

            dve.wait_ge(w_rounded, 1)
            nc.vector.tensor_tensor(w_low[:, :, :], w_raw, bits(w_high[:, :, :]), ALU.subtract).then_inc(w_split, 1)
            split_x(0)

            dve.wait_ge(xn_landed[1], 16)
            ks = slice(XN_K, 2 * XN_K)
            nc.vector.tensor_copy(xn_high[:, ks, :], x_nodes[:, ks, :]).then_inc(xn_rounded[1], 1)
            split_xn(1)
            split_q(0, 0)
            split_k(0, 0, acc)
            split_xn(3)
            maxima(0, 0, 0)
            split_x(1)
            maxima(0, 0, 1)
            for b in range(HEAD):
                for u in range(STEPS):
                    group = b * STEPS + u
                    dve.wait_ge(ax_ready, group + 1)
                    nc.vector.tensor_copy(ax[:, group, :],
                                          acc[:, (u % Y_BANKS) * BANK:(u % Y_BANKS + 1) * BANK]).then_inc(ax_copied, 1)
                    ahead = group + 2
                    if ahead < HEAD * STEPS - 1:
                        maxima(ahead // STEPS, ahead // STEPS, ahead % STEPS)
                    if ahead == HEAD * STEPS - 1:
                        reciprocals(0, 0)
                    if u == 0:
                        split_q(b + 1, (b + 1) % 2)
                    if u == 1:
                        split_k(b + 1, (b + 1) % 2, misc)
                    if u == 2:
                        split_x(b + 2)
            maxima(HEAD - 1, HEAD - 1, STEPS - 1)

            def batch(b, par, scoring, projecting, following):
                if following:
                    reciprocals(b + 1, 1 - par)
                for u in range(STEPS):
                    if scoring:
                        maxima(b + HEAD, par, u)
                    if projecting and u == 0:
                        split_q(b + HEAD + 1, 1 - par)
                    if projecting and u == 1:
                        split_k(b + HEAD + 1, 1 - par, misc)
                residual_and_moments(b)

            with dve.Fori(0, LOOPED // 2) as i:
                for par in range(2):
                    batch(i * 2 + par, par, True, True, True)
            for b in range(LOOPED, B):
                batch(b, b % 2, b + HEAD < B, b + HEAD + 1 < B, b + 1 < B)

        @block.gpsimd
        def _(pool):
            def split_x(batch):
                pool.wait_ge(x_rounded, batch + 1)
                nc.gpsimd.tensor_tensor(x_split[C:P, :], x_raw[C:P, :], bits(x_split[C:P, :]),
                                        ALU.subtract).then_inc(x_split_done, 1)
                pool.wait_ge(x_split_done, batch + 1)

            def divide_ax(b, par):
                pool.wait_ge(recip_done, b + 1)
                nc.gpsimd.tensor_tensor(ax_scaled[:, par, :, :], ax[:, :, bass.ds(b * C, C)],
                                        recip[:, par, :].unsqueeze(2).broadcast_to([P, NCH, C]),
                                        ALU.mult).then_inc(ax_divided, 1)

            def center(b):
                pool.wait_ge(moments_done, b + 1)
                pool.wait_ge(normalized, after(b))
                nc.gpsimd.tensor_tensor(cent[:, :, :], y[:, :, :],
                                        moments[:, :, 0:1].broadcast_to([P, NCH, C]),
                                        ALU.subtract).then_inc(centered, 1)

            def normalize(b):
                pool.wait_ge(var_done, b + 1)
                nc.gpsimd.tensor_tensor(rstd[:, :], var_eps[:, :], neg_half[:, :], ALU.pow).then_inc(rstd_done, 1)
                pool.wait_ge(rstd_done, b + 1)
                pool.wait_ge(centered, after(b + 1))
                pool.wait_ge(out_stored, after(b * 16))
                nc.gpsimd.tensor_tensor(normed[:, :, :], cent[:, :, :],
                                        rstd[:, :].unsqueeze(2).broadcast_to([P, NCH, C]),
                                        ALU.mult).then_inc(normalized, 1)

            nc.gpsimd.memset(neg_half[:, :], -0.5).then_inc(constant_set, 1)
            pool.wait_ge(constant_set, 1)
            for part in range(0, XN_PARTS, 2):
                pool.wait_ge(xn_rounded[part], 1)
                ks = slice(part * XN_K, (part + 1) * XN_K)
                nc.gpsimd.tensor_tensor(xn_low[:, ks, :], x_nodes[:, ks, :], bits(xn_high[:, ks, :]),
                                        ALU.subtract).then_inc(xn_split[part], 1)
            for j in range(NCH):
                pool.wait_ge(adj_rounded, j + 1)
                nc.gpsimd.tensor_tensor(adj_low[:, j % ADJ_BUFS, :], adj_raw[:, j % RAW_ADJ, :],
                                        bits(adj_high[:, j % ADJ_BUFS, :]), ALU.subtract).then_inc(adj_split, 1)
            pool.wait_ge(ax_copied, ax_count(NCH - 1))
            divide_ax(0, 0)

            def batch(b, par, splitting, following):
                if following:
                    pool.wait_ge(aggregated, after(b * STEPS))
                    divide_ax(b + 1, 1 - par)
                if splitting:
                    pool.wait_ge(ax_divided, b + 2)
                    split_x(b + HEAD + 2)
                center(b)
                normalize(b)

            with pool.Fori(0, LOOPED // 2) as i:
                for par in range(2):
                    batch(i * 2 + par, par, True, True)
            for b in range(LOOPED, B):
                batch(b, b % 2, b + HEAD + 2 < B, b + 1 < B)


def kernel(x, adj, L0_gnn_Wq, L0_gnn_bq, L0_gnn_Wk, L0_gnn_bk, L0_gnn_Wv):
    import numpy as np
    import concourse.bacc as bacc
    from concourse.bass_utils import run_bass_kernel_spmd

    def laid(a):
        return np.ascontiguousarray(a)

    def twice(a):
        return np.tile(a, (2, 2))

    x, adj = np.asarray(x), np.asarray(adj)
    arrays = {
        "xT": laid(x.transpose(0, 2, 1)),
        "xn": laid(x.reshape(B, NCH, P, C).transpose(2, 1, 0, 3).reshape(P, NCH, B * C)),
        "adjT": laid(adj.reshape(NCH, P, NCH, P).transpose(0, 3, 2, 1).reshape(NCH, P, NCH * P)),
        "w_all": laid(np.hstack([twice(np.asarray(w).T) for w in (L0_gnn_Wq, L0_gnn_Wk, L0_gnn_Wv)]
                                + [np.tile(np.asarray(v).reshape(C, 1), (2, 1)) for v in (L0_gnn_bq, L0_gnn_bk)])),
    }
    nc = bacc.Bacc("TRN2", target_bir_lowering=False, num_devices=1)
    args = [nc.dram_tensor(name, a.shape, mybir.dt.from_np(a.dtype), kind="ExternalInput").ap()
            for name, a in arrays.items()]
    out = nc.dram_tensor("out", (B, P, NCH * C), F32, kind="ExternalOutput").ap()
    gnn_resnorm_kernel(nc, *args, out)
    r = run_bass_kernel_spmd(nc, [arrays], core_ids=[0])
    got = r.results[0]["out"]
    return laid(got.reshape(B, P, NCH, C).transpose(0, 2, 1, 3).reshape(B, N, C))
```

```python
from contextlib import ExitStack

import concourse.bass as bass
from concourse import mybir

F32 = mybir.dt.float32
F32R = mybir.dt.float32r
ALU = mybir.AluOpType
ACT = mybir.ActivationFunctionType
AX_X = mybir.AxisListType.X

B, N, C = 8, 1024, 64
P = 128
NCH = N // P
BANK = 512
HALVES = N // BANK
STEPS = NCH // 2
EPS = 1e-5

SCORE_BUFS = 2
Y_BANKS = 2
RAW_ADJ = 2
ADJ_BUFS = 2

WARM_UPS = 3

HEAD = 2
LOOPED = B - HEAD - 2
LAST = B - 1
HALF_K = NCH // HALVES


def bits(ap):
    return ap.bitcast(F32)


def gnn_resnorm_kernel(nc: bass.Bass, xT, xn, adjT, w_all, out):
    ctx = ExitStack()
    with ctx:
        def sb(name, shape, dt=F32):
            return ctx.enter_context(nc.sbuf_tensor(name, shape, dt))

        def pb(name, shape):
            return ctx.enter_context(nc.psum_tensor(name, shape, F32))

        def sem(name):
            return ctx.enter_context(nc.semaphore(name))

        weights = sb("weights", [P, P + C + 1])
        w_raw = weights[:, 0:P]
        wv = weights[:, P:P + C]
        bias = weights[:, P + C:P + C + 1]
        w_high = sb("w_high", [P, P], F32R)
        w_low = sb("w_low", [P, P], F32R)
        x_raw = sb("x_raw", [P, N])
        x_split = sb("x_split", [P, N], F32R)
        q_high = sb("q_high", [P, 2, N], F32R)
        q_low = sb("q_low", [P, 2, N], F32R)
        k_split = sb("k_split", [P, 2, N], F32R)
        x_nodes = sb("x_nodes", [P, NCH, B * C])
        xn_high = sb("xn_high", [P, NCH, B * C], F32R)
        xn_low = sb("xn_low", [P, NCH, B * C], F32R)
        adj_raw = sb("adj_raw", [P, RAW_ADJ, NCH * P])
        adj_high = sb("adj_high", [P, ADJ_BUFS, NCH * P], F32R)
        adj_low = sb("adj_low", [P, ADJ_BUFS, NCH * P], F32R)
        ax = sb("ax", [P, NCH, B * C])
        ax_scaled = sb("ax_scaled", [P, 2, NCH, C])
        probs = sb("probs", [P, 2, NCH, N])
        neg_max = sb("neg_max", [P, 2, NCH])
        sums = sb("sums", [P, 2, NCH])
        recip = sb("recip", [P, 2, NCH])
        agg = sb("agg", [P, N])
        y = sb("y", [P, NCH, C])
        cent = sb("cent", [P, NCH, C])
        normed = sb("normed", [P, NCH, C])
        stats = sb("stats", [P, NCH, 6])
        moments = sb("moments", [P, NCH, 2])
        var_eps = sb("var_eps", [P, NCH])
        rstd = sb("rstd", [P, NCH])
        last_var_eps = sb("last_var_eps", [P, NCH])
        last_deviation = sb("last_deviation", [P, NCH])
        last_rstd = sb("last_rstd", [P, NCH])
        neg_half = sb("neg_half", [P, NCH])
        zeros = sb("zeros", [P, BANK])
        start_mark = sb("start_mark", [P, 16])

        scores = [pb(f"scores{i}", [P, N]) for i in range(SCORE_BUFS)]
        acc = pb("acc", [P, N])
        misc = pb("misc", [P, N])

        last_aggregated = [sem(f"last_aggregated{i}") for i in range(HALVES)]
        last_copied = [sem(f"last_copied{i}") for i in range(HALVES)]
        last_mixed = [sem(f"last_mixed{i}") for i in range(HALVES)]
        last_added = [sem(f"last_added{i}") for i in range(HALVES)]
        last_stats = [sem(f"last_stats{i}") for i in range(HALVES)]
        last_moments = [sem(f"last_moments{i}") for i in range(HALVES)]
        last_var = [sem(f"last_var{i}") for i in range(HALVES)]
        last_rooted = [sem(f"last_rooted{i}") for i in range(HALVES)]
        last_rstd_done = [sem(f"last_rstd_done{i}") for i in range(HALVES)]
        last_centered = [sem(f"last_centered{i}") for i in range(HALVES)]
        last_normalized = [sem(f"last_normalized{i}") for i in range(HALVES)]
        w_landed = sem("w_landed")
        x_landed = sem("x_landed")
        xn_landed = [sem(f"xn_landed{i}") for i in range(4)]
        adj_landed = [sem(f"adj_landed{i}") for i in range(RAW_ADJ)]
        q_doubled = [sem(f"q_doubled{i}") for i in range(2)]
        out_stored = sem("out_stored")
        projected = sem("projected")
        scores_ready = sem("scores_ready")
        ax_ready = sem("ax_ready")
        aggregated = sem("aggregated")
        mixed = sem("mixed")
        w_rounded = sem("w_rounded")
        x_rounded = sem("x_rounded")
        xn_rounded = sem("xn_rounded")
        adj_rounded = sem("adj_rounded")
        q_rounded = sem("q_rounded")
        k_rounded = sem("k_rounded")
        exp_done = sem("exp_done")
        agg_copied = sem("agg_copied")
        w_split = sem("w_split")
        zeros_set = sem("zeros_set")
        first_adj_split = sem("first_adj_split")
        last_divided = sem("last_divided")
        xn_split = sem("xn_split")
        q_split = sem("q_split")
        k_split_done = sem("k_split_done")
        max_done = sem("max_done")
        ax_copied = sem("ax_copied")
        recip_done = sem("recip_done")
        residual_added = sem("residual_added")
        stats_done = sem("stats_done")
        moments_done = sem("moments_done")
        var_done = sem("var_done")
        rstd_done = sem("rstd_done")
        constant_set = sem("constant_set")
        x_split_done = sem("x_split_done")
        adj_split = sem("adj_split")
        ax_divided = sem("ax_divided")
        centered = sem("centered")
        normalized = sem("normalized")

        XN_PARTS = len(xn_landed)
        XN_K = NCH // XN_PARTS

        FROM_ONE = (k_split_done, residual_added, agg_copied, scores_ready, mixed, centered,
                    aggregated, normalized, out_stored)

        def after(count):
            return count + 1

        def exp_count(batch, chunks):
            return batch * NCH + (chunks + SCORE_BUFS)

        def ax_count(group):
            return group + (1 + Y_BANKS)

        def half_k(h):
            return slice(h * HALF_K, (h + 1) * HALF_K)

        block = ctx.enter_context(nc.Block())

        @block.sync
        def _(sp):
            def load_x(batch):
                for half in range(2):
                    sp.dma_start(x_raw[half * C:(half + 1) * C, :], xT[batch]).then_inc(x_landed, 16)

            def load_adj(j):
                if j == RAW_ADJ:
                    sp.wait_ge(first_adj_split, 1)
                if j > RAW_ADJ:
                    sp.wait_ge(adj_split, j - RAW_ADJ)
                sp.dma_start(adj_raw[:, j % RAW_ADJ, :], adjT[j]).then_inc(adj_landed[j % RAW_ADJ], 16)

            def double_q(batch, par):
                sp.wait_ge(q_rounded, batch * HALVES + HALVES)
                sp.dma_start(bits(q_high[C:P, par, :]), bits(q_high[0:C, par, :])).then_inc(q_doubled[par], 16)
                sp.wait_ge(q_split, batch * HALVES + HALVES)
                sp.dma_start(bits(q_low[C:P, par, :]), bits(q_low[0:C, par, :])).then_inc(q_doubled[par], 16)

            load_x(0)
            load_adj(0)
            for part in range(XN_PARTS):
                ks = slice(part * XN_K, (part + 1) * XN_K)
                sp.dma_start(x_nodes[:, ks, :], xn[:, ks, :]).then_inc(xn_landed[part], 16)
            load_adj(1)
            sp.wait_ge(x_split_done, 1)
            load_x(1)
            load_adj(2)
            double_q(0, 0)
            load_adj(3)
            sp.wait_ge(x_split_done, 2)
            load_x(2)
            double_q(1, 1)
            load_adj(4)
            load_adj(5)
            sp.wait_ge(x_split_done, 3)
            load_x(3)
            load_adj(6)
            load_adj(7)
            double_q(2, 0)

            def store(b):
                sp.wait_ge(normalized, after(b + 1))
                sp.dma_start(out[b], normed[:, :, :]).then_inc(out_stored, 16)

            with sp.Fori(0, LOOPED // 2) as i:
                for par in range(2):
                    b = i * 2 + par
                    sp.wait_ge(x_split_done, b + HEAD + 2)
                    load_x(b + HEAD + 2)
                    double_q(b + HEAD + 1, 1 - par)
                    store(b)
            for b in range(LOOPED, LAST):
                if b + HEAD + 1 < B:
                    double_q(b + HEAD + 1, 1 - b % 2)
                store(b)
            for h in range(HALVES):
                sp.wait_ge(last_normalized[h], 1)
                sp.dma_start(out[LAST][:, h * HALF_K * C:(h + 1) * HALF_K * C],
                             y[:, half_k(h), :]).then_inc(out_stored, 16)
            sp.wait_ge(out_stored, after(16 * (LAST + HALVES)))

        @block.tensor
        def _(pe):
            def project(batch):
                pe.wait_ge(x_split_done, batch + 1)
                pe.wait_ge(k_split_done, after(batch * HALVES))
                for h in range(HALVES):
                    cols = slice(h * BANK, (h + 1) * BANK)
                    nc.tensor.matmul(misc[:, cols], w_high[:, :], x_split[:, cols],
                                     start=True, stop=False)
                    nc.tensor.matmul(misc[:, cols], w_low[:, :], x_split[:, cols],
                                     start=False, stop=True).then_inc(projected, 1)

            def score(batch, par, u):
                if u == 0:
                    pe.wait_ge(q_doubled[par], (batch - par) * 16 + 32)
                    pe.wait_ge(k_split_done, after(batch * HALVES + HALVES))
                for s in range(2):
                    j = 2 * u + s
                    pe.wait_ge(exp_done, exp_count(batch, j + 1 - SCORE_BUFS))
                    for h in range(HALVES):
                        cols = slice(h * BANK, (h + 1) * BANK)
                        keys = k_split[:, par, j * P:(j + 1) * P]
                        nc.tensor.matmul(scores[s][:, cols], keys, q_high[:, par, cols],
                                         start=True, stop=False)
                        last = nc.tensor.matmul(scores[s][:, cols], keys, q_low[:, par, cols],
                                                start=False, stop=True)
                    last.then_inc(scores_ready, 1)

            def adj_times_x(group, ks=range(NCH)):
                u = group % STEPS
                if group == 0:
                    pe.wait_ge(first_adj_split, 1)
                else:
                    pe.wait_ge(adj_split, group)
                pe.wait_ge(ax_copied, group + 1)
                rows = acc[:, (u % Y_BANKS) * BANK:(u % Y_BANKS + 1) * BANK]
                a, b = adj_high[:, u % ADJ_BUFS, :], adj_low[:, u % ADJ_BUFS, :]
                for k in ks:
                    if group == 0 and k % XN_K == 0:
                        pe.wait_ge(xn_split, k // XN_K + 1)
                    ms = slice(k * P, (k + 1) * P)
                    nc.tensor.matmul(rows, a[:, ms], xn_high[:, k, :], start=(k == 0), stop=False)
                    nc.tensor.matmul(rows, a[:, ms], xn_low[:, k, :], start=False, stop=False)
                    last = nc.tensor.matmul(rows, b[:, ms], xn_high[:, k, :], start=False,
                                            stop=(k == NCH - 1))
                if ks[-1] == NCH - 1:
                    last.then_inc(ax_ready, 1)

            def aggregate(b, par, u, into):
                if u == 0:
                    if into is acc:
                        pe.wait_ge(ax_divided, b + 1)
                    else:
                        pe.wait_ge(last_divided, 1)
                    pe.wait_ge(exp_done, exp_count(b, NCH))
                    if into is acc:
                        pe.wait_ge(agg_copied, after(b))
                for h in range(HALVES):
                    for s in range(2):
                        last = nc.tensor.matmul(
                            into[s * C:(s + 1) * C, h * BANK:(h + 1) * BANK],
                            ax_scaled[:, par, 2 * u + s, :],
                            probs[:, par, 2 * u + s, h * BANK:(h + 1) * BANK],
                            start=(u == 0), stop=(u == STEPS - 1))
                    if into is not acc and u == STEPS - 1:
                        last.then_inc(last_aggregated[h], 1)
                if into is acc:
                    last.then_inc(aggregated, 1)

            def mix(ks, done):
                for k in ks:
                    last = nc.tensor.matmul(misc[:, k * P:k * P + C], agg[:, k * P:(k + 1) * P],
                                            wv, start=True, stop=True)
                last.then_inc(done, 1)

            pe.wait_ge(zeros_set, 1)
            for _ in range(WARM_UPS):
                nc.tensor.matmul(acc[:, 0:BANK], zeros[:, 0:P], zeros[:, :], start=True, stop=True)
            pe.wait_ge(w_split, 1)
            project(0)
            adj_times_x(0)
            for b in range(HEAD):
                for u in range(STEPS):
                    step = b * STEPS + u
                    if step < NCH - 3:
                        adj_times_x(step + 1)
                    if step == NCH - 3:
                        adj_times_x(NCH - 2, range(0, 5))
                    if step == NCH - 2:
                        adj_times_x(NCH - 2, range(5, NCH))
                        adj_times_x(NCH - 1, range(0, 3))
                    if step == NCH - 1:
                        adj_times_x(NCH - 1, range(3, NCH))
                    score(b, b, u)
                    if u == 0:
                        project(b + 1)

            pe.wait_ge(ax_copied, ax_count(NCH - 1))

            def batch(b, par, scoring, projecting):
                for u in range(STEPS):
                    aggregate(b, par, u, acc)
                    if projecting and u == 0:
                        pe.wait_ge(residual_added, after(b))
                        project(b + HEAD + 1)
                    if scoring:
                        score(b + HEAD, par, u)
                if projecting:
                    pe.wait_ge(k_split_done, after((b + HEAD + 2) * HALVES))
                else:
                    pe.wait_ge(residual_added, after(b))
                pe.wait_ge(agg_copied, after(b + 1))
                mix(range(NCH), mixed)

            with pe.Fori(0, LOOPED // 2) as i:
                for par in range(2):
                    batch(i * 2 + par, par, True, True)
            for b in range(LOOPED, LAST - 1):
                batch(b, b % 2, b + HEAD < B, b + HEAD + 1 < B)

            for u in range(STEPS):
                aggregate(LAST - 1, (LAST - 1) % 2, u, acc)
            for u in range(STEPS):
                aggregate(LAST, LAST % 2, u, scores[0])
                if u == 1:
                    pe.wait_ge(residual_added, after(LAST - 1))
                    pe.wait_ge(agg_copied, after(LAST))
                    mix(range(NCH), mixed)
            pe.wait_ge(residual_added, after(LAST))
            for h in range(HALVES):
                pe.wait_ge(last_copied[h], 1)
                mix(range(h * HALF_K, (h + 1) * HALF_K), last_mixed[h])

        @block.scalar
        def _(act):
            act.dma_start(weights[:, :], w_all).then_inc(w_landed, 16)

            def round_x(batch):
                act.wait_ge(x_landed, batch * 32 + 32)
                if not isinstance(batch, int) or batch > 0:
                    act.wait_ge(projected, batch * HALVES)
                nc.scalar.activation(x_split[:, :], x_raw[:, :], ACT.Copy).then_inc(x_rounded, 1)

            def round_q(batch, par):
                for h in range(HALVES):
                    cols = slice(h * BANK, (h + 1) * BANK)
                    act.wait_ge(projected, batch * HALVES + (h + 1))
                    if not isinstance(batch, int) or batch > 1:
                        act.wait_ge(scores_ready, after((batch - 1) * NCH))
                    nc.scalar.activation(q_high[0:C, par, cols], misc[0:C, cols], ACT.Identity,
                                         bias=bias[0:C, :]).then_inc(q_rounded, 1)

            def round_k(batch, par):
                for h in range(HALVES):
                    cols = slice(h * BANK, (h + 1) * BANK)
                    act.wait_ge(projected, batch * HALVES + (h + 1))
                    nc.scalar.activation(k_split[C:P, par, cols], misc[C:P, cols], ACT.Identity,
                                         bias=bias[C:P, :]).then_inc(k_rounded, 1)

            def round_xn(part):
                act.wait_ge(xn_landed[part], 16)
                ks = slice(part * XN_K, (part + 1) * XN_K)
                nc.scalar.activation(xn_high[:, ks, :], x_nodes[:, ks, :], ACT.Copy).then_inc(xn_rounded, 1)

            def round_adj(group):
                act.wait_ge(adj_landed[group % RAW_ADJ], 16 * (group // RAW_ADJ + 1))
                act.wait_ge(ax_copied, group + 1)
                nc.scalar.activation(adj_high[:, group % ADJ_BUFS, :], adj_raw[:, group % RAW_ADJ, :],
                                     ACT.Copy).then_inc(adj_rounded, 1)

            def exps(batch, par, u, aggregating=None):
                if aggregating is not None:
                    act.wait_ge(aggregated, after(aggregating * STEPS + (u + 1)))
                for s in range(2):
                    j = 2 * u + s
                    act.wait_ge(max_done, batch * NCH + (j + 1))
                    nc.scalar.activation(probs[:, par, j, :], scores[s][:, :], ACT.Exp,
                                         bias=neg_max[:, par, j:j + 1],
                                         accum_out=sums[:, par, j:j + 1]).then_inc(exp_done, 1)

            act.wait_ge(w_landed, 16)
            nc.scalar.activation(w_high[:, :], w_raw, ACT.Copy).then_inc(w_rounded, 1)
            round_x(0)
            round_adj(0)
            round_xn(0)
            round_xn(1)
            round_xn(2)
            round_q(0, 0)
            round_xn(3)
            round_adj(1)
            round_k(0, 0)
            round_x(1)
            for b in range(HEAD):
                for u in range(STEPS):
                    if b * STEPS + u + 2 < NCH:
                        round_adj(b * STEPS + u + 2)
                    if u == 0:
                        round_q(b + 1, (b + 1) % 2)
                    if u == 1:
                        round_k(b + 1, (b + 1) % 2)
                    if u == 2:
                        round_x(b + 2)
                    exps(b, b, u)

            def batch(b, par, scoring, projecting, splitting):
                for u in range(STEPS):
                    if u == STEPS - 1:
                        act.wait_ge(aggregated, after(b * STEPS + STEPS))
                        act.wait_ge(mixed, after(b))
                        nc.scalar.activation(agg[:, :], acc[:, :], ACT.Copy).then_inc(agg_copied, 1)
                    if projecting and u == 0:
                        round_q(b + HEAD + 1, 1 - par)
                    if projecting and u == 1:
                        round_k(b + HEAD + 1, 1 - par)
                    if splitting and u == 3:
                        round_x(b + HEAD + 2)
                    if scoring:
                        exps(b + HEAD, par, u, b)

            with act.Fori(0, LOOPED // 2) as i:
                for par in range(2):
                    batch(i * 2 + par, par, True, True, True)
            for b in range(LOOPED, LAST):
                batch(b, b % 2, b + HEAD < B, b + HEAD + 1 < B, b + HEAD + 2 < B)

            act.wait_ge(last_aggregated[0], 1)
            act.wait_ge(mixed, after(LAST))
            nc.scalar.activation(agg[:, 0:BANK], scores[0][:, 0:BANK], ACT.Copy).then_inc(last_copied[0], 1)
            for h in range(HALVES):
                act.wait_ge(last_var[h], 1)
                nc.scalar.activation(last_deviation[:, half_k(h)], last_var_eps[:, half_k(h)],
                                     ACT.Sqrt).then_inc(last_rooted[h], 1)

        @block.vector
        def _(dve):
            def copy_ax(group):
                dve.wait_ge(ax_ready, group + 1)
                bank = group % Y_BANKS
                nc.vector.tensor_copy(ax[:, group, :],
                                      acc[:, bank * BANK:(bank + 1) * BANK]).then_inc(ax_copied, 1)

            nc.vector.memset(zeros[:, :], 0.0).then_inc(zeros_set, 1)
            starts = [exp_done] * SCORE_BUFS + [ax_copied] * Y_BANKS + list(FROM_ONE)
            for n, semaphore in enumerate(starts):
                nc.vector.memset(start_mark[:, n:n + 1], 0.0).then_inc(semaphore, 1)

            def split_q(batch, par):
                for h in range(HALVES):
                    cols = slice(h * BANK, (h + 1) * BANK)
                    dve.wait_ge(q_rounded, batch * HALVES + (h + 1))
                    nc.vector.scalar_tensor_tensor(
                        out=q_low[0:C, par, cols], in0=misc[0:C, cols], scalar=bias[0:C, :],
                        in1=bits(q_high[0:C, par, cols]), op0=ALU.add, op1=ALU.subtract).then_inc(q_split, 1)

            def split_k(batch, par):
                for h in range(HALVES):
                    cols = slice(h * BANK, (h + 1) * BANK)
                    dve.wait_ge(k_rounded, batch * HALVES + (h + 1))
                    nc.vector.scalar_tensor_tensor(
                        out=k_split[0:C, par, cols], in0=misc[C:P, cols], scalar=bias[C:P, :],
                        in1=bits(k_split[C:P, par, cols]), op0=ALU.add, op1=ALU.subtract).then_inc(k_split_done, 1)

            def maxima(batch, par, u):
                for s in range(2):
                    j = 2 * u + s
                    dve.wait_ge(scores_ready, after(batch * NCH + (j + 1)))
                    nc.vector.tensor_reduce(neg_max[:, par, j:j + 1], scores[s][:, :], AX_X, ALU.max,
                                            negate=True).then_inc(max_done, 1)

            def reciprocals(batch, par):
                dve.wait_ge(exp_done, exp_count(batch, NCH))
                nc.vector.reciprocal(recip[:, par, :], sums[:, par, :]).then_inc(recip_done, 1)

            def residual_and_moments(b):
                dve.wait_ge(mixed, after(b + 1))
                dve.wait_ge(centered, after(b))
                nc.vector.tensor_tensor(y[:, :, :], misc[:, :].rearrange("p (k c) -> p k c", k=NCH)[:, :, 0:C],
                                        x_nodes[:, :, bass.ds(b * C, C)], ALU.add).then_inc(residual_added, 1)
                dve.wait_ge(residual_added, after(b + 1))
                for k in range(NCH):
                    last = nc.vector.bn_stats(stats[:, k, :], y[:, k, :])
                last.then_inc(stats_done, 1)
                dve.wait_ge(stats_done, b + 1)
                nc.vector.memset(start_mark[:, 0:1], 0.0)
                for k in range(NCH):
                    last = nc.vector.bn_aggr(moments[:, k, :], stats[:, k, :])
                last.then_inc(moments_done, 1)
                dve.wait_ge(moments_done, b + 1)
                dve.wait_ge(normalized, after(b))
                nc.vector.tensor_scalar(var_eps[:, :], moments[:, :, 1], EPS, None, ALU.add).then_inc(var_done, 1)

            def split_x(batch):
                dve.wait_ge(x_rounded, batch + 1)
                nc.vector.tensor_tensor(x_split[C:P, :], x_raw[C:P, :], bits(x_split[C:P, :]),
                                        ALU.subtract).then_inc(x_split_done, 1)

            def split_xn(part):
                ks = slice(part * XN_K, (part + 1) * XN_K)
                dve.wait_ge(xn_rounded, part + 1)
                nc.vector.tensor_tensor(xn_low[:, ks, :], x_nodes[:, ks, :], bits(xn_high[:, ks, :]),
                                        ALU.subtract).then_inc(xn_split, 1)

            dve.wait_ge(w_rounded, 1)
            nc.vector.tensor_tensor(w_low[:, :], w_raw, bits(w_high[:, :]), ALU.subtract).then_inc(w_split, 1)
            split_x(0)

            dve.wait_ge(adj_rounded, 1)
            nc.vector.tensor_tensor(adj_low[:, 0, :], adj_raw[:, 0, :], bits(adj_high[:, 0, :]),
                                    ALU.subtract).then_inc(first_adj_split, 1)
            for part in range(XN_PARTS):
                split_xn(part)
            split_q(0, 0)
            split_k(0, 0)
            split_x(1)
            copy_ax(0)
            for b in range(HEAD):
                for u in range(STEPS):
                    step = b * STEPS + u
                    if step < NCH - 3:
                        copy_ax(step + 1)
                    if step >= NCH - 2:
                        copy_ax(step)
                    maxima(b, b, u)
                    if u == 0:
                        split_q(b + 1, (b + 1) % 2)
                    if u == 1:
                        split_k(b + 1, (b + 1) % 2)
                    if u == 2:
                        split_x(b + 2)
                        if b == 1:
                            reciprocals(0, 0)

            def batch(b, par, scoring, projecting, following):
                if following:
                    reciprocals(b + 1, 1 - par)
                if isinstance(b, int) and b + 1 == LAST:
                    dve.wait_ge(recip_done, LAST + 1)
                    dve.wait_ge(aggregated, after((LAST - 1) * STEPS))
                    nc.vector.tensor_tensor(ax_scaled[:, LAST % 2, :, :], ax[:, :, LAST * C:B * C],
                                            recip[:, LAST % 2, :].unsqueeze(2).broadcast_to([P, NCH, C]),
                                            ALU.mult).then_inc(last_divided, 1)
                for u in range(STEPS):
                    if scoring:
                        maxima(b + HEAD, par, u)
                    if projecting and u == 0:
                        split_q(b + HEAD + 1, 1 - par)
                    if projecting and u == 1:
                        split_k(b + HEAD + 1, 1 - par)
                residual_and_moments(b)

            with dve.Fori(0, LOOPED // 2) as i:
                for par in range(2):
                    batch(i * 2 + par, par, True, True, True)
            for b in range(LOOPED, LAST):
                batch(b, b % 2, b + HEAD < B, b + HEAD + 1 < B, b + 1 < B)

            dve.wait_ge(last_aggregated[1], 1)
            dve.wait_ge(mixed, after(LAST))
            nc.vector.tensor_copy(agg[:, BANK:N], scores[0][:, BANK:N]).then_inc(last_copied[1], 1)
            dve.wait_ge(centered, after(LAST))

            def last_add(h):
                ks = half_k(h)
                dve.wait_ge(last_mixed[h], 1)
                nc.vector.tensor_tensor(y[:, ks, :], misc[:, :].rearrange("p (k c) -> p k c", k=NCH)[:, ks, 0:C],
                                        x_nodes[:, ks, LAST * C:B * C], ALU.add).then_inc(last_added[h], 1)

            def last_variance(h):
                dve.wait_ge(last_added[h], 1)
                for k in range(h * HALF_K, (h + 1) * HALF_K):
                    last = nc.vector.bn_stats(stats[:, k, :], y[:, k, :])
                last.then_inc(last_stats[h], 1)
                dve.wait_ge(last_stats[h], 1)
                for k in range(h * HALF_K, (h + 1) * HALF_K):
                    last = nc.vector.bn_aggr(moments[:, k, :], stats[:, k, :])
                last.then_inc(last_moments[h], 1)
                dve.wait_ge(last_moments[h], 1)
                nc.vector.tensor_scalar(last_var_eps[:, half_k(h)], moments[:, half_k(h), 1], EPS, None,
                                        ALU.add).then_inc(last_var[h], 1)

            def last_reciprocal(h):
                dve.wait_ge(last_rooted[h], 1)
                nc.vector.reciprocal(last_rstd[:, half_k(h)],
                                     last_deviation[:, half_k(h)]).then_inc(last_rstd_done[h], 1)

            last_add(0)
            last_variance(0)
            last_add(1)
            last_reciprocal(0)
            last_variance(1)
            ks = half_k(1)
            nc.vector.tensor_tensor(y[:, ks, :], y[:, ks, :], moments[:, ks, 0:1].broadcast_to([P, HALF_K, C]),
                                    ALU.subtract).then_inc(last_centered[1], 1)
            last_reciprocal(1)
            dve.wait_ge(last_rstd_done[1], 1)
            dve.wait_ge(last_centered[1], 1)
            nc.vector.tensor_tensor(y[:, ks, :], y[:, ks, :],
                                    last_rstd[:, ks].unsqueeze(2).broadcast_to([P, HALF_K, C]),
                                    ALU.mult).then_inc(last_normalized[1], 1)

        @block.gpsimd
        def _(pool):
            def split_x(batch):
                pool.wait_ge(x_rounded, batch + 1)
                nc.gpsimd.tensor_tensor(x_split[C:P, :], x_raw[C:P, :], bits(x_split[C:P, :]),
                                        ALU.subtract).then_inc(x_split_done, 1)
                pool.wait_ge(x_split_done, batch + 1)

            def divide_ax(b, par):
                pool.wait_ge(recip_done, b + 1)
                nc.gpsimd.tensor_tensor(ax_scaled[:, par, :, :], ax[:, :, bass.ds(b * C, C)],
                                        recip[:, par, :].unsqueeze(2).broadcast_to([P, NCH, C]),
                                        ALU.mult).then_inc(ax_divided, 1)

            def center(b):
                pool.wait_ge(moments_done, b + 1)
                pool.wait_ge(normalized, after(b))
                nc.gpsimd.tensor_tensor(cent[:, :, :], y[:, :, :],
                                        moments[:, :, 0:1].broadcast_to([P, NCH, C]),
                                        ALU.subtract).then_inc(centered, 1)

            def normalize(b):
                pool.wait_ge(var_done, b + 1)
                nc.gpsimd.tensor_tensor(rstd[:, :], var_eps[:, :], neg_half[:, :], ALU.pow).then_inc(rstd_done, 1)
                pool.wait_ge(rstd_done, b + 1)
                pool.wait_ge(centered, after(b + 1))
                pool.wait_ge(out_stored, after(b * 16))
                nc.gpsimd.tensor_tensor(normed[:, :, :], cent[:, :, :],
                                        rstd[:, :].unsqueeze(2).broadcast_to([P, NCH, C]),
                                        ALU.mult).then_inc(normalized, 1)

            nc.gpsimd.memset(neg_half[:, :], -0.5).then_inc(constant_set, 1)
            pool.wait_ge(constant_set, 1)
            for j in range(1, NCH):
                pool.wait_ge(adj_rounded, j + 1)
                nc.gpsimd.tensor_tensor(adj_low[:, j % ADJ_BUFS, :], adj_raw[:, j % RAW_ADJ, :],
                                        bits(adj_high[:, j % ADJ_BUFS, :]), ALU.subtract).then_inc(adj_split, 1)
            pool.wait_ge(ax_copied, ax_count(NCH - 1))
            divide_ax(0, 0)

            def batch(b, par, splitting, following):
                if following:
                    pool.wait_ge(aggregated, after(b * STEPS))
                    divide_ax(b + 1, 1 - par)
                if splitting:
                    pool.wait_ge(ax_divided, b + 2)
                    split_x(b + HEAD + 2)
                center(b)
                normalize(b)

            with pool.Fori(0, LOOPED // 2) as i:
                for par in range(2):
                    batch(i * 2 + par, par, True, True)
            for b in range(LOOPED, LAST):
                batch(b, b % 2, b + HEAD + 2 < B, b + 1 < LAST)

            ks = half_k(0)
            pool.wait_ge(last_moments[0], 1)
            nc.gpsimd.tensor_tensor(y[:, ks, :], y[:, ks, :], moments[:, ks, 0:1].broadcast_to([P, HALF_K, C]),
                                    ALU.subtract).then_inc(last_centered[0], 1)
            pool.wait_ge(last_rstd_done[0], 1)
            pool.wait_ge(last_centered[0], 1)
            nc.gpsimd.tensor_tensor(y[:, ks, :], y[:, ks, :],
                                    last_rstd[:, ks].unsqueeze(2).broadcast_to([P, HALF_K, C]),
                                    ALU.mult).then_inc(last_normalized[0], 1)


def kernel(x, adj, L0_gnn_Wq, L0_gnn_bq, L0_gnn_Wk, L0_gnn_bk, L0_gnn_Wv):
    import numpy as np
    import concourse.bacc as bacc
    from concourse.bass_utils import run_bass_kernel_spmd

    def laid(a):
        return np.ascontiguousarray(a)

    x, adj = np.asarray(x), np.asarray(adj)
    arrays = {
        "xT": laid(x.transpose(0, 2, 1)),
        "xn": laid(x.reshape(B, NCH, P, C).transpose(2, 1, 0, 3).reshape(P, NCH, B * C)),
        "adjT": laid(adj.reshape(NCH, P, NCH, P).transpose(0, 3, 2, 1).reshape(NCH, P, NCH * P)),
        "w_all": laid(np.hstack([
            np.tile(np.hstack([np.asarray(L0_gnn_Wq).T, np.asarray(L0_gnn_Wk).T]), (2, 1)),
            np.tile(np.asarray(L0_gnn_Wv).T, (2, 1)),
            np.hstack([np.asarray(L0_gnn_bq), np.asarray(L0_gnn_bk)]).reshape(P, 1)])),
    }
    nc = bacc.Bacc("TRN2", target_bir_lowering=False, num_devices=1)
    args = [nc.dram_tensor(name, a.shape, mybir.dt.from_np(a.dtype), kind="ExternalInput").ap()
            for name, a in arrays.items()]
    out = nc.dram_tensor("out", (B, P, NCH * C), F32, kind="ExternalOutput").ap()
    gnn_resnorm_kernel(nc, *args, out)
    r = run_bass_kernel_spmd(nc, [arrays], core_ids=[0])
    got = r.results[0]["out"]
    return laid(got.reshape(B, P, NCH, C).transpose(0, 2, 1, 3).reshape(B, N, C))
```
